# Optimizing a Trainium2 kernel written in Bass

```python
import numpy as np
import jax
import jax.numpy as jnp

def _softmax(x, axis=-1):
    return jax.nn.softmax(x, axis=axis)

def _gelu(x):
    return jax.nn.gelu(x, approximate=True)

def _silu(x):
    return jax.nn.silu(x)

def _sigmoid(x):
    return jax.nn.sigmoid(x)

def _layernorm(x, axis=-1, eps=1e-05):
    m = jnp.mean(x, axis=axis, keepdims=True)
    v = jnp.var(x, axis=axis, keepdims=True)
    return (x - m) / jnp.sqrt(v + eps)

def _scatter_add(tgt, idx, src, axis=0):
    return tgt.at[idx].add(src)

def _segment_sum(src, seg, n):
    return jax.ops.segment_sum(src, seg, n)
kernel_name = 'mk_adj_resnorm_d2_adj_r2_2051e1'

def setup_inputs(seed: int=0):
    np.random.seed(seed)
    _w = jnp.asarray

    def _rec_inputs():
        import jax
        import jax.numpy as jnp
        _gk = jax.random.key(seed)
        x = -0.000929 + 1 * jax.random.normal(jax.random.fold_in(_gk, 1), (8192, 64), jnp.float32)
        _a = jax.random.bernoulli(jax.random.fold_in(_gk, 2), 0.000976562, (8192, 8192))
        _a = jnp.logical_or(_a, jnp.swapaxes(_a, -1, -2))
        _a = jnp.logical_or(_a, jnp.eye(8192, dtype=bool))
        _af = _a.astype(jnp.float32)
        _af = _af * jax.random.uniform(jax.random.fold_in(_gk, 3), (8192, 8192), jnp.float32, 0.05, 0.0423436)
        adj = _af
        return (x, adj)
    x, adj = _rec_inputs()

    def _L0_gnn_setup():
        import jax, jax.numpy as jnp
        import numpy as np
        N, F_IN, F_OUT, K = (8192, 64, 64, 3)
        key = jax.random.key(seed)
        k1, k2, k3, k4 = jax.random.split(key, 4)
        x = jax.random.normal(k1, (N, F_IN), dtype=jnp.float32)
        L_tilde = jax.random.normal(k2, (N, N), dtype=jnp.float32) / np.float32(np.sqrt(N))
        stdv = 1.0 / np.sqrt(F_OUT)
        weights = jax.random.uniform(k3, (K + 1, F_IN, F_OUT), dtype=jnp.float32, minval=-stdv, maxval=stdv)
        bias = jax.random.uniform(k4, (F_OUT,), dtype=jnp.float32, minval=-stdv, maxval=stdv)
        return {'x': x, 'L_tilde': L_tilde, 'weights': weights, 'bias': bias}
    _L0_gnn_all = _L0_gnn_setup()
    _L0_gnn_in = {k: v for k, v in _L0_gnn_all.items() if k in ('weights', 'bias')}
    del _L0_gnn_all

    def _L1_gnn_setup():
        import jax, jax.numpy as jnp
        import numpy as np
        N = 5000
        DIM = 64
        F_CONST = 1.0
        B_CONST = 0.1
        R_CONST = 0.01
        key = jax.random.key(seed)
        k1, k2 = jax.random.split(key)
        t = jnp.zeros((1,), dtype=jnp.float32)
        x = jax.random.uniform(k1, (N, DIM), dtype=jnp.float32)
        A = jax.random.uniform(k2, (N, N), dtype=jnp.float32)
        return {'t': t, 'x': x, 'A': A}
    _L1_gnn_all = _L1_gnn_setup()
    _L1_gnn_in = {k: v for k, v in _L1_gnn_all.items() if k in ('t',)}
    del _L1_gnn_all
    return {'x': x, 'adj': adj, 'L0_gnn_weights': _L0_gnn_in['weights'], 'L0_gnn_bias': _L0_gnn_in['bias'], 'L1_gnn_t': _L1_gnn_in['t']}

def reference(x, adj, L0_gnn_weights, L0_gnn_bias, L1_gnn_t):
    import jax
    import jax.numpy as jnp

    def _L0_gnn_ref(x, L_tilde, weights, bias):
        import jax, jax.numpy as jnp
        import numpy as np
        N, F_IN, F_OUT, K = (8192, 64, 64, 3)
        T_prev = x
        out = T_prev @ weights[0]
        T_curr = L_tilde @ x
        out = out + T_curr @ weights[1]
        for k in range(2, K + 1):
            T_next = 2.0 * (L_tilde @ T_curr) - T_prev
            out = out + T_next @ weights[k]
            T_prev, T_curr = (T_curr, T_next)
        return out + bias

    def _L1_gnn_ref(t, x, A):
        import jax, jax.numpy as jnp
        import numpy as np
        N = 5000
        DIM = 64
        F_CONST = 1.0
        B_CONST = 0.1
        R_CONST = 0.01
        Ax = A @ x
        outer = R_CONST * jnp.sum(x * Ax, axis=1, keepdims=True)
        return F_CONST - B_CONST * x - outer
    x = _layernorm(x + _L0_gnn_ref(x, adj, L0_gnn_weights, L0_gnn_bias), axis=-1)
    x = _layernorm(x + _L1_gnn_ref(L1_gnn_t, x, adj), axis=-1)
    return x

_drawn_inputs = setup_inputs


def setup_inputs(seed=0):
    import zlib

    import numpy as np

    out = dict(_drawn_inputs(seed))
    spreads = {}
    factors = {}
    for name, (base, spread) in spreads.items():
        noise = np.random.default_rng([zlib.crc32(name.encode()), seed]).standard_normal(out[name].shape)
        drawn = base * np.exp(spread * noise) if base else spread * noise
        out[name] = jnp.asarray(drawn.astype(out[name].dtype))
    for name, factor in factors.items():
        out[name] = (out[name] * factor).astype(out[name].dtype)
    return out
```

```python
from contextlib import ExitStack

import concourse.bass as bass
from concourse import mybir

P = 128
ALU = mybir.AluOpType
F32 = mybir.dt.float32
ACT = mybir.ActivationFunctionType
AX_X = mybir.AxisListType.X

SLOTS = 4
CUT = 6
EPS = 1e-5
F_CONST, B_CONST, R_CONST = 1.0, 0.1, 0.01
DOWN, UP2, DOWN3, LAST = range(4)
NOW = (0, 1, 0, 1)


class Row:

    def __init__(self, sweep, r, n, before):
        self.sweep, self.r, self.n, self.before = sweep, r, n, before
        short = n if isinstance(n, int) else CUT
        needed = short - 2 if sweep in (UP2, DOWN3) else short - 1
        self.close_at = max(0, min(2, needed))
        self.use_at = max(0, min(4, needed))


def rows(eng, nb):
    yield Row(DOWN, 0, nb, None)
    with eng.Fori(1, nb) as r:
        yield Row(DOWN, r, nb, (DOWN, r - 1))
    before = (DOWN, nb - 1)
    for n in range(1, CUT):
        yield Row(UP2, nb - n, n, before)
        before = (UP2, nb - n)
    with eng.Fori(CUT, nb + 1) as n:
        yield Row(UP2, nb - n, n, (UP2, nb + 1 - n))
    before = (UP2, 0)
    for n in range(1, CUT):
        yield Row(DOWN3, n - 1, n, before)
        before = (DOWN3, n - 1)
    with eng.Fori(CUT, nb + 1) as n:
        yield Row(DOWN3, n - 1, n, (DOWN3, n - 2))
    yield Row(LAST, 0, nb, (DOWN3, nb - 1))
    with eng.Fori(1, nb - CUT + 1) as r:
        yield Row(LAST, r, nb - r, (LAST, r - 1))
    for n in range(CUT - 1, 0, -1):
        yield Row(LAST, nb - n, n, (LAST, nb - n - 1))


def blocks(eng, row, split):
    if isinstance(row.n, int) and row.n <= split:
        yield from range(row.n)
        return
    yield from range(split)
    with eng.Fori(split, row.n) as k:
        yield k


def chebyshev_program(nc: bass.Bass, a_blocks, x_rows, x_cols, weights, bias, out):
    nb, _, _, _, wide = a_blocks.shape
    tiles = wide // P
    feat = x_cols.shape[0]
    assert feat == 64 and wide == 512 and nb % SLOTS == 0
    row_count = 4 * nb

    with ExitStack() as ctx:
        def sb(name, shape):
            return ctx.enter_context(nc.sbuf_tensor(name, shape, F32))

        def psum(name, shape):
            return ctx.enter_context(nc.psum_tensor(name, shape, F32))

        def sem(name):
            return ctx.enter_context(nc.semaphore(name))

        a_ring = sb("a_ring", [P, SLOTS, tiles * wide])
        operand = sb("operand", [P, nb, tiles, 2, feat])
        staged_op = sb("staged_op", [P, tiles, 2 * feat])
        cols = sb("cols", [P, nb, wide])
        natural = sb("natural", [P, nb, tiles, feat])
        turn_in = sb("turn_in", [P, wide])
        zero = sb("zero", [P, tiles, feat])
        bias_all = sb("bias_all", [P, feat])
        turn_w = sb("turn_w", [P, 3, P])
        h = sb("h", [P, tiles, feat])
        sq = sb("sq", [P, tiles, feat])
        stat = sb("stat", [P, 2, tiles])

        acc = psum("acc", [P, 2, wide])
        turned = psum("turned", [P, tiles, P])

        s_x = sem("s_x")
        s_const = sem("s_const")
        s_ident = sem("s_ident")
        s_opinit = sem("s_opinit")
        s_slot = [sem(f"s_slot{i}") for i in range(SLOTS)]
        s_landed = sem("s_landed")
        s_staged = sem("s_staged")
        s_tile = sem("s_tile")
        s_turnin = sem("s_turnin")
        s_turned = sem("s_turned")
        s_row = sem("s_row")
        s_var = sem("s_var")
        s_std = sem("s_std")
        s_out = sem("s_out")

        block = ctx.enter_context(nc.Block())

        @block.sync
        def _(sp):
            quads = sp.alloc_register("quads")
            former = sp.alloc_register("former")
            row_at = sp.alloc_register("row_at")
            col_at = sp.alloc_register("col_at")
            edge = sp.alloc_register("edge")
            for reg in (quads, former, row_at, col_at, edge):
                sp.reg_mov(reg, 0)

            def step(sweep):
                if sweep == DOWN:
                    sp.reg_add(col_at, col_at, 1)
                    sp.reg_alu(col_at, col_at, nb, op=ALU.mod)
                    sp.reg_alu(edge, col_at, row_at, op=ALU.is_equal)
                    sp.reg_add(row_at, row_at, edge)
                    sp.reg_add(col_at, col_at, edge)
                    sp.reg_alu(col_at, col_at, nb, op=ALU.mod)
                elif sweep == UP2:
                    sp.reg_alu(edge, col_at, row_at, op=ALU.is_equal)
                    sp.reg_alu(row_at, row_at, edge, op=ALU.subtract)
                    sp.reg_alu(edge, edge, nb, op=ALU.mult)
                    sp.reg_alu(col_at, col_at, 1, op=ALU.subtract)
                    sp.reg_alu(col_at, col_at, edge, op=ALU.max)
                    sp.reg_alu(col_at, col_at, nb - 1, op=ALU.min)
                elif sweep == DOWN3:
                    sp.reg_alu(edge, col_at, row_at, op=ALU.is_equal)
                    sp.reg_add(col_at, col_at, 1)
                    sp.reg_add(row_at, row_at, edge)
                    sp.reg_alu(edge, edge, -nb, op=ALU.mult)
                    sp.reg_add(col_at, col_at, edge)
                    sp.reg_alu(col_at, col_at, 0, op=ALU.max)
                else:
                    sp.reg_add(col_at, col_at, 1)
                    sp.reg_alu(edge, col_at, nb, op=ALU.is_equal)
                    sp.reg_add(row_at, row_at, edge)
                    sp.reg_alu(edge, edge, row_at, op=ALU.mult)
                    sp.reg_alu(col_at, col_at, nb, op=ALU.mod)
                    sp.reg_add(col_at, col_at, edge)

            def quad(sweep, first=False):
                q = sp.snap(quads, min_val=0, max_val=(nb * nb * 4) // SLOTS)
                f = sp.snap(former, min_val=0, max_val=(nb * nb * 4) // SLOTS)
                for s in range(SLOTS):
                    if not first or s == SLOTS - 1:
                        oldest = (s + 1) % SLOTS
                        sp.wait_ge(s_slot[oldest], 16 * (q if oldest else q + 1))
                        sp.sem_inc(s_landed, 1)
                    if not first:
                        sp.wait_ge(s_tile, f * (SLOTS * tiles) + (s + 1) * tiles)
                    r = sp.snap(row_at, min_val=0, max_val=nb - 1)
                    c = sp.snap(col_at, min_val=0, max_val=nb - 1)
                    sp.dma_start(a_ring[:, s, :],
                                 a_blocks[r, c].rearrange("p t i -> p (t i)")).then_inc(s_slot[s], 16)
                    step(sweep)
                sp.reg_add(quads, quads, 1)
                if not first:
                    sp.reg_add(former, former, 1)

            quad(DOWN, first=True)
            with sp.Fori(1, nb * nb // SLOTS) as _q:
                quad(DOWN)
            tri = nb * (nb + 1) // 2 // SLOTS
            for sweep, start in ((UP2, (nb - 1, nb - 1)), (DOWN3, (0, 0)), (LAST, (0, 0))):
                sp.reg_mov(row_at, start[0])
                sp.reg_mov(col_at, start[1])
                with sp.Fori(0, tri) as _q:
                    quad(sweep)
            total = nb * nb // SLOTS + 3 * tri
            for s in range(1, SLOTS):
                sp.wait_ge(s_slot[s], 16 * total)
                sp.sem_inc(s_landed, 1)
            sp.wait_ge(s_out, 16 * nb)

        @block.scalar
        def _(act):
            for c in range(4):
                part = slice(c * nb // 4, (c + 1) * nb // 4)
                act.dma_start(natural[:, part], x_rows[:, part]).then_inc(s_x, 16)
            act.dma_start(cols[feat:P], x_cols.rearrange("f (b i) -> f b i", i=wide)).then_inc(s_const, 16)
            act.wait_ge(s_ident, 3)
            act.dma_start(turn_w[0:feat, 0, 0:feat], weights[1]).then_inc(s_const, 16)
            act.dma_start(turn_w[feat:P, 0, 0:feat], weights[0]).then_inc(s_const, 16)
            act.dma_start(turn_w[0:feat, 2, 0:feat], weights[3]).then_inc(s_const, 16)
            act.dma_start(turn_w[feat:P, 2, 0:feat], weights[2]).then_inc(s_const, 16)
            act.dma_start(bias_all[:, :], bias.rearrange("(a f) -> a f", a=1).broadcast_to([P, feat])
                          ).then_inc(s_const, 16)
            def root(count):
                act.wait_ge(s_var, count)
                nc.scalar.activation(stat[:, 1, :], stat[:, 1, :], ACT.Sqrt).then_inc(s_std, 1)

            with act.Fori(0, nb) as r:
                root(r + 1)
            with act.Fori(0, nb) as r:
                root(r + (nb + 1))
                act.wait_ge(s_row, r + (3 * nb + 1))
                act.dma_start(out[r], natural[:, r]).then_inc(s_out, 16)

        @block.gpsimd
        def _(pool):
            nc.gpsimd.memset(zero[:], 0.0)
            nc.gpsimd.memset(turn_w[:], 0.0).then_inc(s_ident, 1)
            pool.wait_ge(s_ident, 1)
            nc.gpsimd.affine_select(out=turn_w[:, 0, feat:P], in_=turn_w[:, 0, feat:P],
                                    compare_op=ALU.not_equal, fill=1.0, base=0,
                                    pattern=[[-1, feat]], channel_multiplier=1).then_inc(s_ident, 1)
            nc.gpsimd.affine_select(out=turn_w[:, 1, feat:P], in_=turn_w[:, 1, feat:P],
                                    compare_op=ALU.not_equal, fill=1.0, base=-feat,
                                    pattern=[[-1, feat]], channel_multiplier=1).then_inc(s_ident, 1)
            former = pool.alloc_register("former")
            row_no = pool.alloc_register("row_no")
            col_at = pool.alloc_register("col_at")
            pool.reg_mov(former, 0)
            pool.reg_mov(row_no, 0)
            pool.wait_ge(s_opinit, 1)

            def stage(col, first):
                f = pool.snap(former, min_val=0, max_val=nb * nb * 4 * tiles)
                for t in range(tiles):
                    if not first:
                        pool.wait_ge(s_tile, f + (t + 1))
                    nc.gpsimd.tensor_copy(staged_op[:, t, :],
                                          operand[:, col, t].rearrange("p s f -> p (s f)")
                                          ).then_inc(s_staged, 1)
                if not first:
                    pool.reg_add(former, former, tiles)

            started = False
            for row in rows(pool, nb):
                number = pool.snap(row_no, min_val=0, max_val=row_count)
                for k in blocks(pool, row, row.use_at + 1):
                    if isinstance(k, int) and k == 0 and row.sweep in (UP2, DOWN3):
                        pool.drain()
                        nc.gpsimd.tensor_copy(operand[:, row.r, :, 1 - NOW[row.sweep], :], zero[:])
                        pool.drain()
                    if row.sweep == DOWN:
                        col = (row.r + k) % nb
                    elif row.sweep == UP2:
                        col = (nb - 1) - k
                    elif row.sweep == DOWN3:
                        col = k
                    else:
                        col = row.r + k
                    pool.reg_mov(col_at, col)
                    col = pool.snap(col_at, min_val=0, max_val=nb - 1)
                    if isinstance(k, int) and k == row.use_at and row.before:
                        pool.wait_ge(s_row, number)
                    stage(col, first=not started)
                    started = True
                pool.reg_add(row_no, row_no, 1)

        @block.tensor
        def _(pe):
            block_no = pe.alloc_register("block_no")
            slot_no = pe.alloc_register("slot_no")
            row_no = pe.alloc_register("row_no")
            rows_off = pe.alloc_register("rows_off")
            for reg in (block_no, slot_no, row_no, rows_off):
                pe.reg_mov(reg, 0)

            def multiply(bank, first):
                b = pe.snap(block_no, min_val=0, max_val=nb * nb * 4)
                slot = pe.snap(slot_no, min_val=0, max_val=SLOTS - 1)
                pe.wait_ge(s_landed, b + 1)
                for t in range(tiles):
                    pe.wait_ge(s_staged, b * tiles + (t + 1))
                    nc.tensor.matmul(acc[:, bank, :], staged_op[:, t, :],
                                     a_ring[:, slot, t * wide:(t + 1) * wide],
                                     start=first and t == 0, stop=False,
                                     skip_group_check=True).then_inc(s_tile, 1)
                pe.reg_add(block_no, block_no, 1)
                pe.reg_add(slot_no, slot_no, 1)
                pe.reg_alu(slot_no, slot_no, SLOTS, op=ALU.mod)

            def turn(sweep, number):
                pe.wait_ge(s_turnin, number)
                kind = {DOWN: 0, UP2: 1, DOWN3: 2, LAST: 1}[sweep]
                for t in range(tiles):
                    last = nc.tensor.matmul(turned[:, t, :], turn_in[:, t * P:(t + 1) * P],
                                            turn_w[:, kind, :], start=True, stop=True)
                last.then_inc(s_turned, 1)

            for row in rows(pe, nb):
                number = pe.snap(row_no, min_val=0, max_val=row_count)
                bank = number % 2
                if row.before:
                    pe.wait_ge(s_row, pe.snap(rows_off, min_val=0, max_val=row_count))
                    pe.reg_add(rows_off, rows_off, 1)
                for k in blocks(pe, row, max(1, row.close_at + 1)):
                    if isinstance(k, int) and k == row.close_at and row.before:
                        turn(row.before[0], number)
                    multiply(bank, isinstance(k, int) and k == 0)
                pe.reg_add(row_no, row_no, 1)
            turn(LAST, row_count)

        @block.vector
        def _(dve):
            dve.wait_ge(s_x, 64)
            nc.vector.memset(operand[:, :, :, 1, :], 0.0)
            nc.vector.tensor_copy(operand[:, :, :, 0, :], natural[:]).then_inc(s_opinit, 1)
            nc.vector.memset(turn_in[:], 0.0)
            dve.drain()
            dve.wait_ge(s_const, 6 * 16)
            dve.wait_ge(s_ident, 3)

            block_no = dve.alloc_register("block_no")
            row_no = dve.alloc_register("row_no")
            norm_no = dve.alloc_register("norm_no")
            length = dve.alloc_register("length")
            count = dve.alloc_register("count")
            dve.reg_mov(norm_no, 0)
            dve.reg_mov(block_no, 0)
            dve.drain()
            dve.reg_mov(row_no, 0)
            halves = (slice(0, feat), slice(feat, P))

            def layer_norm(dst, src):
                mean, var = stat[:, 0, :], stat[:, 1, :]
                dve.drain()
                nc.vector.tensor_reduce(out=mean, in_=src, op=ALU.add, axis=AX_X)
                dve.drain()
                nc.vector.tensor_scalar(mean, mean, 1.0 / feat, None, ALU.mult)
                dve.drain()
                nc.vector.tensor_tensor(src, src, mean.unsqueeze(2).broadcast_to([P, tiles, feat]),
                                        ALU.subtract)
                dve.drain()
                nc.vector.tensor_tensor(sq[:], src, src, ALU.mult)
                dve.drain()
                nc.vector.tensor_reduce(out=var, in_=sq[:], op=ALU.add, axis=AX_X)
                dve.drain()
                nc.vector.tensor_scalar(var, var, 1.0 / feat, EPS, ALU.mult, ALU.add).then_inc(s_var, 1)
                dve.reg_add(norm_no, norm_no, 1)
                dve.wait_ge(s_std, dve.snap(norm_no, min_val=1, max_val=2 * nb))
                nc.vector.reciprocal(var, var)
                dve.drain()
                return nc.vector.tensor_tensor(dst, src, var.unsqueeze(2).broadcast_to([P, tiles, feat]),
                                               ALU.mult)

            def close(sweep, r, number):
                now = NOW[sweep]
                mine, other = halves[now], halves[1 - now]
                bank = (number + 1) % 2
                if sweep == DOWN:
                    nc.vector.tensor_copy(turn_in[other], cols[other, r])
                    nc.vector.tensor_copy(turn_in[mine], acc[mine, bank]).then_inc(s_turnin, 1)
                    dve.drain()
                    nc.vector.tensor_copy(cols[mine, r], turn_in[mine])
                    nc.vector.scalar_tensor_tensor(out=cols[other, r], in0=acc[other, bank], scalar=2.0,
                                                   in1=cols[other, r], op0=ALU.mult, op1=ALU.subtract)
                elif sweep == UP2:
                    nc.vector.scalar_tensor_tensor(out=turn_in[mine], in0=acc[mine, bank], scalar=2.0,
                                                   in1=cols[mine, r], op0=ALU.mult, op1=ALU.add
                                                   ).then_inc(s_turnin, 1)
                    dve.drain()
                    nc.vector.tensor_copy(cols[mine, r], turn_in[mine])
                    nc.vector.scalar_tensor_tensor(out=cols[other, r], in0=acc[other, bank], scalar=2.0,
                                                   in1=cols[other, r], op0=ALU.mult, op1=ALU.subtract)
                elif sweep == DOWN3:
                    nc.vector.tensor_copy(turn_in[other], cols[other, r])
                    nc.vector.scalar_tensor_tensor(out=turn_in[mine], in0=acc[mine, bank], scalar=2.0,
                                                   in1=cols[mine, r], op0=ALU.mult, op1=ALU.add
                                                   ).then_inc(s_turnin, 1)
                    dve.drain()
                    nc.vector.tensor_copy(cols[other, r], acc[other, bank])
                else:
                    nc.vector.tensor_tensor(turn_in[mine], acc[mine, bank], cols[mine, r], ALU.add
                                            ).then_inc(s_turnin, 1)
                dve.wait_ge(s_turned, number)
                by_rows = turned[:, :, feat:P]
                share = turned[:, :, 0:feat]
                if sweep == DOWN:
                    nc.vector.tensor_copy(operand[:, r, :, 1 - now, :], by_rows)
                    nc.vector.tensor_tensor(natural[:, r], natural[:, r], share, ALU.add
                                            ).then_inc(s_row, 1)
                elif sweep == UP2:
                    nc.vector.tensor_copy(operand[:, r, :, 1 - now, :], by_rows).then_inc(s_row, 1)
                elif sweep == DOWN3:
                    nc.vector.tensor_tensor(h[:], natural[:, r], share, ALU.add)
                    dve.drain()
                    nc.vector.tensor_tensor(h[:], h[:], bias_all[:].unsqueeze(1).broadcast_to([P, tiles, feat]),
                                            ALU.add)
                    layer_norm(natural[:, r], h[:])
                    dve.drain()
                    nc.vector.tensor_copy(operand[:, r, :, 1 - now, :], natural[:, r]).then_inc(s_row, 1)
                else:
                    outer = stat[:, 0, :]
                    nc.vector.tensor_tensor(sq[:], natural[:, r], by_rows, ALU.mult)
                    dve.drain()
                    nc.vector.tensor_reduce(out=outer, in_=sq[:], op=ALU.add, axis=AX_X)
                    dve.drain()
                    nc.vector.tensor_scalar(outer, outer, R_CONST, None, ALU.mult)
                    nc.vector.tensor_scalar(h[:], natural[:, r], -B_CONST, F_CONST, ALU.mult, ALU.add)
                    dve.drain()
                    nc.vector.tensor_tensor(h[:], h[:], outer.unsqueeze(2).broadcast_to([P, tiles, feat]),
                                            ALU.subtract)
                    dve.drain()
                    nc.vector.tensor_tensor(h[:], h[:], natural[:, r], ALU.add)
                    layer_norm(natural[:, r], h[:]).then_inc(s_row, 1)

            for row in rows(dve, nb):
                dve.drain()
                dve.reg_mov(length, row.n)
                dve.reg_alu(count, length, 1, op=ALU.max)
                dve.reg_add(block_no, block_no, count)
                dve.reg_add(row_no, row_no, 1)
                tiles_by = dve.snap(block_no, min_val=1, max_val=nb * nb * 4)
                number = dve.snap(row_no, min_val=1, max_val=row_count)
                dve.wait_ge(s_tile, tiles_by * tiles)
                close(row.sweep, row.r, number)


def kernel(x, adj, L0_gnn_weights, L0_gnn_bias, L1_gnn_t):
    import numpy as np
    import concourse.bacc as bacc
    from concourse.bass_utils import run_bass_kernel_spmd

    n, feat = x.shape
    wide = 512
    nb, tiles = n // wide, wide // P
    adj, x = np.asarray(adj), np.asarray(x)
    a_blocks = np.ascontiguousarray(
        adj.reshape(nb, wide, nb, tiles, P).transpose(0, 2, 4, 3, 1))
    x_rows = np.ascontiguousarray(x.reshape(nb, tiles, P, feat).transpose(2, 0, 1, 3))
    arrays = {"a_blocks": a_blocks, "x_rows": x_rows, "x_cols": np.ascontiguousarray(x.T),
              "weights": np.ascontiguousarray(L0_gnn_weights), "bias": np.ascontiguousarray(L0_gnn_bias)}
    nc = bacc.Bacc("TRN2", target_bir_lowering=False, num_devices=1)
    args = [nc.dram_tensor(k, v.shape, F32, kind="ExternalInput").ap() for k, v in arrays.items()]
    out = nc.dram_tensor("out", (nb, P, tiles, feat), F32, kind="ExternalOutput").ap()
    chebyshev_program(nc, *args, out)
    result = run_bass_kernel_spmd(nc, [arrays], core_ids=[0])
    got = result.results[0]["out"]
    return np.ascontiguousarray(got.transpose(0, 2, 1, 3).reshape(n, feat))
```

```python
from contextlib import ExitStack

import concourse.bass as bass
from concourse import mybir

P = 128
ALU = mybir.AluOpType
F32 = mybir.dt.float32
F32R = mybir.dt.float32r
ACT = mybir.ActivationFunctionType
AX_X = mybir.AxisListType.X

SLOTS = 4
CUT = 6
EPS = 1e-5
F_CONST, B_CONST, R_CONST = 1.0, 0.1, 0.01
DOWN, UP2, DOWN3, LAST = range(4)
NOW = (0, 1, 0, 1)
DIAGONAL = (DOWN, DOWN3)


class Row:

    def __init__(self, sweep, r, n, before):
        self.sweep, self.r, self.n, self.before = sweep, r, n, before
        self.diagonal = sweep in DIAGONAL
        latest = max(0, (n if isinstance(n, int) else CUT) - 1)
        self.turn_at = min(2, latest)
        self.use_at = min(4, latest)


def rows(eng, nb):
    yield Row(DOWN, 0, nb - 1, None)
    with eng.Fori(1, nb) as r:
        yield Row(DOWN, r, nb - 1, (DOWN, r - 1))
    before = (DOWN, nb - 1)
    for n in range(CUT):
        yield Row(UP2, nb - 1 - n, n, before)
        before = (UP2, nb - 1 - n)
    with eng.Fori(CUT, nb) as n:
        yield Row(UP2, (nb - 1) - n, n, (UP2, nb - n))
    before = (UP2, 0)
    for n in range(CUT):
        yield Row(DOWN3, n, n, before)
        before = (DOWN3, n)
    with eng.Fori(CUT, nb - 1) as n:
        yield Row(DOWN3, n, n, (DOWN3, n - 1))
    yield Row(DOWN3, nb - 1, nb - 1, (DOWN3, nb - 2))
    yield Row(LAST, 0, nb - 1, (DOWN3, nb - 1))
    with eng.Fori(1, nb - CUT) as r:
        yield Row(LAST, r, (nb - 1) - r, (LAST, r - 1))
    for n in range(CUT - 1, -1, -1):
        yield Row(LAST, nb - 1 - n, n, (LAST, nb - 2 - n))


def blocks(eng, row):
    first = row.use_at + 1
    if isinstance(row.n, int) and row.n <= first:
        yield from range(max(1, row.n))
        return
    yield from range(first)
    with eng.Fori(first, row.n) as k:
        yield k


def at(k, position):
    return isinstance(k, int) and k == position


def column(row, k, nb):
    if row.sweep == DOWN:
        return (row.r + 1 + k) % nb
    if row.sweep == UP2:
        return (nb - 1) - k
    if row.sweep == DOWN3:
        return k
    return row.r + 1 + k


class Count:

    def __init__(self, eng, name, top, start=0):
        self.eng, self.top = eng, top
        self.reg = eng.alloc_register(name)
        eng.reg_mov(self.reg, start)

    def value(self):
        return self.eng.snap(self.reg, min_val=0, max_val=self.top)

    def add(self, by=1):
        self.eng.reg_add(self.reg, self.reg, by)


def chebyshev_program(nc: bass.Bass, a_blocks, x_rows, x_cols, weights, bias, out):
    nb, _, _, _, wide = a_blocks.shape
    tiles = wide // P
    half = tiles // 2
    feat = x_cols.shape[0]
    off_diagonal = nb * (nb - 1)
    assert feat == 64 and wide == 512 and (off_diagonal // 2) % SLOTS == 0
    many = 4 * nb * nb * tiles

    with ExitStack() as ctx:
        def sb(name, shape, dtype=F32):
            return ctx.enter_context(nc.sbuf_tensor(name, shape, dtype))

        def psum(name, shape):
            return ctx.enter_context(nc.psum_tensor(name, shape, F32))

        def sem(name):
            return ctx.enter_context(nc.semaphore(name))

        a_ring = sb("a_ring", [P, SLOTS, tiles * wide])
        a_diag = sb("a_diag", [P, 2, tiles * wide])
        a_high = sb("a_high", [P, 2, tiles * wide], F32R)
        a_low = sb("a_low", [P, 2, tiles * wide], F32R)
        operand = sb("operand", [P, nb, tiles, 2, 2, feat], F32R)
        staged = sb("staged", [P, tiles, 2, 2 * feat], F32R)
        cols = sb("cols", [P, nb, wide])
        natural = sb("natural", [P, nb, tiles, feat])
        turn_in = sb("turn_in", [P, wide])
        zero = sb("zero", [P, wide])
        bias_all = sb("bias_all", [P, feat])
        turn_w = sb("turn_w", [P, 3, P])
        h = sb("h", [P, tiles, feat])
        sq = sb("sq", [P, tiles, feat])
        stat = sb("stat", [P, 2, tiles])

        acc = psum("acc", [P, 2, wide])
        turned = psum("turned", [P, tiles, P])

        s_x = [sem(f"s_x{c}") for c in range(4)]
        s_const = sem("s_const")
        s_ident = sem("s_ident")
        s_opinit = sem("s_opinit")
        s_slot = [sem(f"s_slot{i}") for i in range(SLOTS)]
        s_landed = sem("s_landed")
        s_diag = sem("s_diag")
        s_high = sem("s_high")
        s_low = sem("s_low")
        s_high_d = sem("s_high_d")
        s_low_d = sem("s_low_d")
        s_staged_a = sem("s_staged_a")
        s_staged_p = sem("s_staged_p")
        s_tile = sem("s_tile")
        s_zeroed = sem("s_zeroed")
        s_turnin = sem("s_turnin")
        s_turned = sem("s_turned")
        s_result = sem("s_result")
        s_bank = sem("s_bank")
        s_var = sem("s_var")
        s_std = sem("s_std")
        s_out = sem("s_out")

        block = ctx.enter_context(nc.Block())

        @block.sync
        def _(sp):
            quads = Count(sp, "quads", many)
            former = Count(sp, "former", many)
            row_at, col_at, edge = (sp.alloc_register(name) for name in ("row_at", "col_at", "edge"))
            sp.reg_mov(row_at, 0)
            sp.reg_mov(col_at, 1)

            def step(sweep):
                if sweep == DOWN:
                    sp.reg_add(col_at, col_at, 1)
                    sp.reg_alu(col_at, col_at, nb, op=ALU.mod)
                    sp.reg_alu(edge, col_at, row_at, op=ALU.is_equal)
                    sp.reg_add(row_at, row_at, edge)
                    sp.reg_add(col_at, col_at, edge)
                    sp.reg_add(col_at, col_at, edge)
                    sp.reg_alu(col_at, col_at, nb, op=ALU.mod)
                elif sweep == UP2:
                    sp.reg_alu(col_at, col_at, 1, op=ALU.subtract)
                    sp.reg_alu(edge, col_at, row_at, op=ALU.is_equal)
                    sp.reg_alu(row_at, row_at, edge, op=ALU.subtract)
                    sp.reg_alu(row_at, row_at, 0, op=ALU.max)
                    sp.reg_alu(edge, edge, nb, op=ALU.mult)
                    sp.reg_alu(col_at, col_at, edge, op=ALU.max)
                    sp.reg_alu(col_at, col_at, nb - 1, op=ALU.min)
                elif sweep == DOWN3:
                    sp.reg_add(col_at, col_at, 1)
                    sp.reg_alu(edge, col_at, row_at, op=ALU.is_equal)
                    sp.reg_add(row_at, row_at, edge)
                    sp.reg_alu(edge, edge, -nb, op=ALU.mult)
                    sp.reg_add(col_at, col_at, edge)
                    sp.reg_alu(col_at, col_at, 0, op=ALU.max)
                else:
                    sp.reg_add(col_at, col_at, 1)
                    sp.reg_alu(edge, col_at, nb, op=ALU.is_equal)
                    sp.reg_add(row_at, row_at, edge)
                    sp.reg_alu(col_at, col_at, nb, op=ALU.mod)
                    sp.reg_alu(edge, edge, row_at, op=ALU.mult)
                    sp.reg_add(col_at, col_at, edge)
                    sp.reg_alu(edge, edge, 1, op=ALU.min)
                    sp.reg_add(col_at, col_at, edge)

            def quad(sweep, first=False):
                q, f = quads.value(), former.value()
                for s in range(SLOTS):
                    if not first or s == SLOTS - 1:
                        oldest = (s + 1) % SLOTS
                        sp.wait_ge(s_slot[oldest], 16 * (q if oldest else q + 1))
                        sp.sem_inc(s_landed, 1)
                    if not first:
                        sp.wait_ge(s_low, f * (SLOTS * 2) + (s + 1) * 2)
                    r = sp.snap(row_at, min_val=0, max_val=nb - 1)
                    c = sp.snap(col_at, min_val=0, max_val=nb - 1)
                    sp.dma_start(a_ring[:, s, :],
                                 a_blocks[r, c].rearrange("p t i -> p (t i)")).then_inc(s_slot[s], 16)
                    step(sweep)
                quads.add()
                if not first:
                    former.add()

            quad(DOWN, first=True)
            with sp.Fori(1, off_diagonal // SLOTS) as _q:
                quad(DOWN)
            triangle = off_diagonal // 2 // SLOTS
            for sweep, start in ((UP2, (nb - 2, nb - 1)), (DOWN3, (1, 0)), (LAST, (0, 1))):
                sp.reg_mov(row_at, start[0])
                sp.reg_mov(col_at, start[1])
                with sp.Fori(0, triangle) as _q:
                    quad(sweep)
            for s in range(1, SLOTS):
                sp.wait_ge(s_slot[s], 16 * (off_diagonal // SLOTS + 3 * triangle))
                sp.sem_inc(s_landed, 1)
            sp.wait_ge(s_out, 16 * nb)

        @block.scalar
        def _(act):
            def load_diagonal(r, place):
                act.dma_start(a_diag[:, place, :], a_blocks[r, r].rearrange("p t i -> p (t i)")
                              ).then_inc(s_diag, 16)

            for c in range(4):
                part = slice(c * nb // 4, (c + 1) * nb // 4)
                act.dma_start(natural[:, part], x_rows[:, part]).then_inc(s_x[c], 16)
            act.dma_start(cols[feat:P], x_cols.rearrange("f (b i) -> f b i", i=wide)).then_inc(s_const, 16)
            load_diagonal(0, 0)
            act.dma_start(bias_all[:, :], bias.rearrange("(a f) -> a f", a=1).broadcast_to([P, feat])
                          ).then_inc(s_const, 16)
            act.wait_ge(s_ident, 3)
            act.dma_start(turn_w[0:feat, 0, 0:feat], weights[1]).then_inc(s_const, 16)
            act.dma_start(turn_w[feat:P, 0, 0:feat], weights[0]).then_inc(s_const, 16)
            act.dma_start(turn_w[0:feat, 2, 0:feat], weights[3]).then_inc(s_const, 16)
            act.dma_start(turn_w[feat:P, 2, 0:feat], weights[2]).then_inc(s_const, 16)

            total = Count(act, "total", many)
            ring = Count(act, "ring", many)
            slot_no = Count(act, "slot_no", SLOTS - 1)
            diag = Count(act, "diag", many)
            loads = Count(act, "loads", many)
            closed = Count(act, "closed", many)
            norms = Count(act, "norms", many)
            freed = Count(act, "freed", many)
            tile_freed = Count(act, "tile_freed", many)
            col_at = act.alloc_register("col_at")
            handled = [0]

            def round_block(source, ready, done):
                high = a_high[:, total.value() % 2, :]
                for g in range(2):
                    if handled[0] >= 2:
                        act.wait_ge(s_tile, freed.value() + (g + 1) * half)
                    if g == 0:
                        act.wait_ge(*ready())
                    part = slice(g * half * wide, (g + 1) * half * wide)
                    act.activation(high[:, part], source[:, part], ACT.Copy).then_inc(done, 1)
                if handled[0] >= 2:
                    freed.add(tiles)

            def stage():
                col = act.snap(col_at, min_val=0, max_val=nb - 1)
                for t in range(half):
                    if handled[0] >= 1:
                        act.wait_ge(s_tile, tile_freed.value() + (t + 1))
                    act.activation(staged[:, t].rearrange("p a f -> p (a f)"),
                                   operand[:, col, t].rearrange("p a s f -> p (a s f)"), ACT.Copy
                                   ).then_inc(s_staged_a, 1)
                if handled[0] >= 1:
                    tile_freed.add(tiles)
                total.add()
                handled[0] += 1

            def diagonal_block(first):
                if first:
                    loads.add()
                place = (loads.value() + 1) % 2
                round_block(a_diag[:, place, :], lambda: (s_diag, 16 * loads.value()), s_high_d)
                diag.add()

            for row in rows(act, nb):
                for k in blocks(act, row):
                    if at(k, row.use_at) and row.before:
                        sweep, before = row.before
                        if sweep in (DOWN3, LAST):
                            norms.add()
                            act.wait_ge(s_var, norms.value())
                            act.activation(stat[:, 1, :], stat[:, 1, :], ACT.Sqrt).then_inc(s_std, 1)
                        if sweep in DIAGONAL:
                            diagonal_block(first=False)
                            act.reg_mov(col_at, before)
                        closed.add()
                        act.wait_ge(s_result, closed.value())
                        if sweep in DIAGONAL:
                            stage()
                        if sweep == LAST:
                            act.dma_start(out[before], natural[:, before]).then_inc(s_out, 16)
                    if at(row.n, 0):
                        break
                    if handled[0] == 0:
                        act.wait_ge(s_opinit, 1)
                    slot = slot_no.value()
                    round_block(a_ring[:, slot, :], lambda: (s_landed, ring.value() + 1), s_high)
                    act.reg_mov(col_at, column(row, k, nb))
                    stage()
                    ring.add()
                    slot_no.add()
                    act.reg_alu(slot_no.reg, slot_no.reg, SLOTS, op=ALU.mod)
                if row.diagonal:
                    split_before = diag.value()
                    diagonal_block(first=True)
                    act.reg_mov(col_at, row.r)
                    stage()
                    if not (row.sweep == DOWN3 and at(row.r, nb - 1)):
                        act.reg_mov(col_at, (row.r + 1) % nb)
                        if row.before:
                            act.wait_ge(s_low_d, split_before * 2)
                        load_diagonal(act.snap(col_at, min_val=0, max_val=nb - 1), loads.value() % 2)
            norms.add()
            act.wait_ge(s_var, norms.value())
            act.activation(stat[:, 1, :], stat[:, 1, :], ACT.Sqrt).then_inc(s_std, 1)
            closed.add()
            act.wait_ge(s_result, closed.value())
            act.dma_start(out[nb - 1], natural[:, nb - 1]).then_inc(s_out, 16)

        @block.gpsimd
        def _(pool):
            nc.gpsimd.memset(zero[:], 0.0)
            nc.gpsimd.memset(turn_w[:], 0.0).then_inc(s_ident, 1)
            pool.wait_ge(s_ident, 1)
            nc.gpsimd.affine_select(out=turn_w[:, 0, feat:P], in_=turn_w[:, 0, feat:P],
                                    compare_op=ALU.not_equal, fill=1.0, base=0,
                                    pattern=[[-1, feat]], channel_multiplier=1).then_inc(s_ident, 1)
            nc.gpsimd.affine_select(out=turn_w[:, 1, feat:P], in_=turn_w[:, 1, feat:P],
                                    compare_op=ALU.not_equal, fill=1.0, base=-feat,
                                    pattern=[[-1, feat]], channel_multiplier=1).then_inc(s_ident, 1)
            closed = Count(pool, "closed", many)
            tile_freed = Count(pool, "tile_freed", many)
            col_at = pool.alloc_register("col_at")
            handled = [0]
            pool.wait_ge(s_opinit, 1)

            def wait_for_result():
                pool.wait_ge(s_result, closed.value())

            def stage():
                col = pool.snap(col_at, min_val=0, max_val=nb - 1)
                for t in range(half, tiles):
                    if handled[0] >= 1:
                        pool.wait_ge(s_tile, tile_freed.value() + (t + 1))
                    nc.gpsimd.tensor_copy(staged[:, t].rearrange("p a f -> p (a f)"),
                                          operand[:, col, t].rearrange("p a s f -> p (a s f)")
                                          ).then_inc(s_staged_p, 1)
                if handled[0] >= 1:
                    tile_freed.add(tiles)
                handled[0] += 1

            for row in rows(pool, nb):
                for k in blocks(pool, row):
                    if at(k, row.use_at) and row.before:
                        sweep, before = row.before
                        closed.add()
                        if sweep in DIAGONAL:
                            pool.reg_mov(col_at, before)
                            wait_for_result()
                            stage()
                    if at(row.n, 0):
                        break
                    pool.reg_mov(col_at, column(row, k, nb))
                    if at(k, row.use_at) and row.before and row.before[0] not in DIAGONAL:
                        wait_for_result()
                    stage()
                if row.diagonal:
                    pool.reg_mov(col_at, row.r)
                    if at(row.n, 0) and row.before:
                        wait_for_result()
                    stage()

        @block.tensor
        def _(pe):
            total = Count(pe, "total", many)
            ring = Count(pe, "ring", many)
            diag = Count(pe, "diag", many)
            row_no = Count(pe, "row_no", many)
            banks = Count(pe, "banks", many, start=1)

            def multiply(bank, start, on_diagonal=False):
                x = total.value()
                high, low = a_high[:, x % 2, :], a_low[:, x % 2, :]
                count, split = (diag, s_low_d) if on_diagonal else (ring, s_low)
                y = count.value()
                for t in range(tiles):
                    if t % half == 0:
                        pe.wait_ge(split, y * 2 + (t // half + 1))
                    pe.wait_ge(s_staged_a if t < half else s_staged_p, x * half + (t % half + 1))
                    part = slice(t * wide, (t + 1) * wide)
                    nc.tensor.matmul(acc[:, bank, :], staged[:, t, 0, :], high[:, part],
                                     start=start and t == 0, stop=False, skip_group_check=True)
                    nc.tensor.matmul(acc[:, bank, :], staged[:, t, 0, :], low[:, part],
                                     start=False, stop=False, skip_group_check=True)
                    nc.tensor.matmul(acc[:, bank, :], staged[:, t, 1, :], high[:, part],
                                     start=False, stop=False, skip_group_check=True).then_inc(s_tile, 1)
                total.add()
                count.add()

            def turn(sweep, number):
                pe.wait_ge(s_turnin, number)
                kind = {DOWN: 0, UP2: 1, DOWN3: 2, LAST: 1}[sweep]
                for t in range(tiles):
                    last = nc.tensor.matmul(turned[:, t, :], turn_in[:, t * P:(t + 1) * P],
                                            turn_w[:, kind, :], start=True, stop=True)
                last.then_inc(s_turned, 1)

            for row in rows(pe, nb):
                number = row_no.value()
                bank, bank_before = number % 2, (number + 1) % 2
                if row.before:
                    pe.wait_ge(s_bank, banks.value())
                    banks.add()
                for k in blocks(pe, row):
                    if at(k, row.turn_at) and row.before:
                        turn(row.before[0], number)
                    if at(k, row.use_at) and row.before and row.before[0] in DIAGONAL:
                        multiply(bank_before, False, on_diagonal=True)
                    if at(row.n, 0):
                        break
                    multiply(bank, at(k, 0))
                if row.diagonal:
                    multiply(bank, at(row.n, 0), on_diagonal=True)
                elif at(row.n, 0):
                    nc.tensor.matmul(acc[:, bank, :], zero[:, 0:P], zero[:, :], start=True, stop=False,
                                     skip_group_check=True).then_inc(s_zeroed, 1)
                row_no.add()
            turn(LAST, 4 * nb)

        @block.vector
        def _(dve):
            nc.vector.memset(operand[:, :, :, :, 1, :].bitcast(F32), 0.0)
            for c in range(4):
                part = slice(c * nb // 4, (c + 1) * nb // 4)
                dve.wait_ge(s_x[c], 16)
                nc.vector.tensor_copy(operand[:, part, :, 0, 0, :], natural[:, part])
                dve.drain()
                last = nc.vector.tensor_tensor(operand[:, part, :, 1, 0, :], natural[:, part],
                                               operand[:, part, :, 0, 0, :], ALU.subtract)
            last.then_inc(s_opinit, 1)
            dve.sem_inc(s_bank, 1)

            total = Count(dve, "total", many)
            ring = Count(dve, "ring", many)
            slot_no = Count(dve, "slot_no", SLOTS - 1)
            diag = Count(dve, "diag", many)
            loads = Count(dve, "loads", many)
            row_no = Count(dve, "row_no", many)
            norms = Count(dve, "norms", many)
            halves = (slice(0, feat), slice(feat, P))

            def split_block(source, count, ready, done):
                x, y = total.value(), count.value()
                for g in range(2):
                    part = slice(g * half * wide, (g + 1) * half * wide)
                    dve.wait_ge(ready, y * 2 + (g + 1))
                    nc.vector.tensor_tensor(a_low[:, x % 2, part], source[:, part],
                                            a_high[:, x % 2, part], ALU.subtract).then_inc(done, 1)
                total.add()
                count.add()

            def layer_norm(dst, src):
                mean, var = stat[:, 0, :], stat[:, 1, :]
                nc.vector.tensor_reduce(out=mean, in_=src, op=ALU.add, axis=AX_X)
                dve.drain()
                nc.vector.tensor_scalar(mean, mean, 1.0 / feat, None, ALU.mult)
                dve.drain()
                nc.vector.tensor_tensor(src, src, mean.unsqueeze(2).broadcast_to([P, tiles, feat]),
                                        ALU.subtract)
                dve.drain()
                nc.vector.tensor_tensor(sq[:], src, src, ALU.mult)
                dve.drain()
                nc.vector.tensor_reduce(out=var, in_=sq[:], op=ALU.add, axis=AX_X)
                dve.drain()
                nc.vector.tensor_scalar(var, var, 1.0 / feat, EPS, ALU.mult, ALU.add).then_inc(s_var, 1)
                norms.add()
                dve.wait_ge(s_std, norms.value())
                nc.vector.reciprocal(var, var)
                dve.drain()
                return nc.vector.tensor_tensor(dst, src, var.unsqueeze(2).broadcast_to([P, tiles, feat]),
                                               ALU.mult)

            def gather_result(sweep, r, bank):
                now = NOW[sweep]
                mine, other = halves[now], halves[1 - now]
                if sweep in DIAGONAL:
                    nc.vector.tensor_copy(turn_in[other], cols[other, r])
                if sweep == DOWN:
                    nc.vector.tensor_copy(turn_in[mine], acc[mine, bank]).then_inc(s_turnin, 1)
                elif sweep == LAST:
                    nc.vector.tensor_tensor(turn_in[mine], acc[mine, bank], cols[mine, r], ALU.add
                                            ).then_inc(s_turnin, 1)
                else:
                    nc.vector.scalar_tensor_tensor(out=turn_in[mine], in0=acc[mine, bank], scalar=2.0,
                                                   in1=cols[mine, r], op0=ALU.mult, op1=ALU.add
                                                   ).then_inc(s_turnin, 1)

            def store_operand(r, side, value):
                nc.vector.tensor_copy(operand[:, r, :, 0, side, :], value)
                dve.drain()
                return nc.vector.tensor_tensor(operand[:, r, :, 1, side, :], value,
                                               operand[:, r, :, 0, side, :], ALU.subtract)

            def store_result(sweep, r, number):
                dve.wait_ge(s_turned, number)
                side = 1 - NOW[sweep]
                by_rows, share = turned[:, :, feat:P], turned[:, :, 0:feat]
                if sweep == DOWN:
                    nc.vector.tensor_tensor(natural[:, r], natural[:, r], share, ALU.add)
                    store_operand(r, side, by_rows).then_inc(s_result, 1)
                elif sweep == UP2:
                    store_operand(r, side, by_rows).then_inc(s_result, 1)
                elif sweep == DOWN3:
                    nc.vector.tensor_tensor(h[:], natural[:, r], share, ALU.add)
                    dve.drain()
                    nc.vector.tensor_tensor(h[:], h[:], bias_all[:].unsqueeze(1).broadcast_to([P, tiles, feat]),
                                            ALU.add)
                    dve.drain()
                    layer_norm(natural[:, r], h[:])
                    dve.drain()
                    store_operand(r, side, natural[:, r]).then_inc(s_result, 1)
                else:
                    outer = stat[:, 0, :]
                    nc.vector.tensor_tensor(sq[:], natural[:, r], by_rows, ALU.mult)
                    nc.vector.tensor_scalar(h[:], natural[:, r], -B_CONST, F_CONST, ALU.mult, ALU.add)
                    dve.drain()
                    nc.vector.tensor_reduce(out=outer, in_=sq[:], op=ALU.add, axis=AX_X)
                    dve.drain()
                    nc.vector.tensor_scalar(outer, outer, R_CONST, None, ALU.mult)
                    dve.drain()
                    nc.vector.tensor_tensor(h[:], h[:], outer.unsqueeze(2).broadcast_to([P, tiles, feat]),
                                            ALU.subtract)
                    dve.drain()
                    nc.vector.tensor_tensor(h[:], h[:], natural[:, r], ALU.add)
                    dve.drain()
                    layer_norm(natural[:, r], h[:]).then_inc(s_result, 1)

            def keep_sums(sweep, r, bank):
                now = NOW[sweep]
                mine, other = halves[now], halves[1 - now]
                if sweep in (DOWN, UP2):
                    nc.vector.scalar_tensor_tensor(out=cols[other, r], in0=acc[other, bank], scalar=2.0,
                                                   in1=cols[other, r], op0=ALU.mult, op1=ALU.subtract)
                    nc.vector.tensor_copy(cols[mine, r], turn_in[mine]).then_inc(s_bank, 1)
                elif sweep == DOWN3:
                    nc.vector.tensor_copy(cols[other, r], acc[other, bank]).then_inc(s_bank, 1)
                else:
                    dve.sem_inc(s_bank, 1)

            for row in rows(dve, nb):
                number = row_no.value()
                bank_before = (number + 1) % 2
                blocks_before = total.value()
                multiplied = blocks_before
                for k in blocks(dve, row):
                    if at(k, row.turn_at) and row.before:
                        sweep, before = row.before
                        dve.drain()
                        if sweep in (UP2, LAST) and at(before, nb - 1):
                            dve.wait_ge(s_zeroed, 1)
                        else:
                            dve.wait_ge(s_tile, blocks_before * tiles)
                        if sweep == DOWN:
                            dve.wait_ge(s_const, 6 * 16)
                        gather_result(sweep, before, bank_before)
                    if at(k, row.use_at) and row.before:
                        sweep, before = row.before
                        if row.sweep == DOWN3:
                            nc.vector.tensor_copy(operand[:, row.r, :, :, 1, :],
                                                  zero[:].rearrange("p (t a f) -> p t a f", a=2, f=feat))
                            dve.drain()
                        store_result(sweep, before, number)
                        if sweep in DIAGONAL:
                            place = (loads.value() + 1) % 2
                            split_block(a_diag[:, place, :], diag, s_high_d, s_low_d)
                            multiplied = total.value()
                    if at(row.n, 0):
                        break
                    split_block(a_ring[:, slot_no.value(), :], ring, s_high, s_low)
                    slot_no.add()
                    dve.reg_alu(slot_no.reg, slot_no.reg, SLOTS, op=ALU.mod)
                if row.diagonal:
                    loads.add()
                    place = (loads.value() + 1) % 2
                    split_block(a_diag[:, place, :], diag, s_high_d, s_low_d)
                if row.before:
                    if row.before[0] in DIAGONAL:
                        dve.wait_ge(s_tile, multiplied * tiles)
                    keep_sums(*row.before, bank_before)
                row_no.add()
            dve.drain()
            dve.wait_ge(s_zeroed, 2)
            gather_result(LAST, nb - 1, (4 * nb + 1) % 2)
            store_result(LAST, nb - 1, 4 * nb)


def kernel(x, adj, L0_gnn_weights, L0_gnn_bias, L1_gnn_t):
    import numpy as np
    import concourse.bacc as bacc
    from concourse.bass_utils import run_bass_kernel_spmd

    n, feat = x.shape
    wide = 512
    nb, tiles = n // wide, wide // P
    adj, x = np.asarray(adj), np.asarray(x)
    a_blocks = np.ascontiguousarray(
        adj.reshape(nb, wide, nb, tiles, P).transpose(0, 2, 4, 3, 1))
    x_rows = np.ascontiguousarray(x.reshape(nb, tiles, P, feat).transpose(2, 0, 1, 3))
    arrays = {"a_blocks": a_blocks, "x_rows": x_rows, "x_cols": np.ascontiguousarray(x.T),
              "weights": np.ascontiguousarray(L0_gnn_weights), "bias": np.ascontiguousarray(L0_gnn_bias)}
    nc = bacc.Bacc("TRN2", target_bir_lowering=False, num_devices=1)
    args = [nc.dram_tensor(k, v.shape, F32, kind="ExternalInput").ap() for k, v in arrays.items()]
    out = nc.dram_tensor("out", (nb, P, tiles, feat), F32, kind="ExternalOutput").ap()
    chebyshev_program(nc, *args, out)
    result = run_bass_kernel_spmd(nc, [arrays], core_ids=[0])
    got = result.results[0]["out"]
    return np.ascontiguousarray(got.transpose(0, 2, 1, 3).reshape(n, feat))
```

```python
from contextlib import ExitStack

import concourse.bass as bass
from concourse import mybir

P = 128
ALU = mybir.AluOpType
F32 = mybir.dt.float32
F32R = mybir.dt.float32r
ACT = mybir.ActivationFunctionType
AX_X = mybir.AxisListType.X

SLOTS = 4
CUT = (0, 6, 9, 9)
TURN, STEPS = 2, (1, 0, 3, 3)
SHORT = 4
SPREAD = 3
OWED_STEPS = STEPS[3]
EPS = 1e-5
F_CONST, B_CONST, R_CONST = 1.0, 0.1, 0.01
DOWN, UP2, DOWN3, LAST = range(4)
NOW = (0, 1, 0, 1)
DIAGONAL = (DOWN, DOWN3)


SPLIT_HALVES = (2, 2, 2, 1)


ORDER = ((0, 1, 2, 3),) * 3 + ((2, 3, 0, 1),)


class Row:

    def __init__(self, sweep, r, n, before, store=None):
        self.sweep, self.r, self.n, self.before = sweep, r, n, before
        self.store = store
        self.postpone, self.owed = False, None
        self.diagonal = sweep in DIAGONAL
        latest = n if isinstance(n, int) else CUT[sweep]
        if sweep != LAST:
            latest = max(0, latest - 1)
        steps = STEPS[before[0]] if before else 0
        turn = 1 if sweep != LAST and latest < SHORT else TURN
        self.turn_at = min(turn, latest)
        self.work_at = tuple(min(turn + 1 + k, latest) for k in range(steps))
        self.close_at = min(turn + 1 + steps, latest)
        self.use_at = min(self.close_at + 1, latest) if sweep != LAST else self.close_at
        self.keep_at = self.use_at if before and sweep != LAST and self.close_at != self.use_at else None
        urgent = sweep != LAST and self.close_at == latest and isinstance(n, int) and n > 0
        self.round_first = urgent or (sweep == LAST and isinstance(n, int) and n < CUT[LAST])
        self.diagonal_at = latest if urgent and sweep == DOWN3 else None
        self.split_first = urgent and sweep == UP2


def rows(eng, nb):
    yield Row(DOWN, 0, nb - 1, None)
    with eng.Fori(1, nb) as r:
        yield Row(DOWN, r, nb - 1, (DOWN, r - 1))
    before = (DOWN, nb - 1)
    for n in range(CUT[UP2]):
        yield Row(UP2, nb - 1 - n, n, before)
        before = (UP2, nb - 1 - n)
    with eng.Fori(CUT[UP2], nb) as n:
        yield Row(UP2, (nb - 1) - n, n, (UP2, nb - n))
    before = (UP2, 0)
    for n in range(CUT[DOWN3]):
        yield Row(DOWN3, n, n, before)
        before = (DOWN3, n)
    with eng.Fori(CUT[DOWN3], nb - 1) as n:
        yield Row(DOWN3, n, n, (DOWN3, n - 1))
    yield Row(DOWN3, nb - 1, nb - 1, (DOWN3, nb - 2))
    before, store, owed = (DOWN3, nb - 1), None, None
    for index, r in enumerate(last_head(nb) + [SPREAD]):
        row = Row(LAST, r, (nb - 1) - r, before, store)
        row.owed = owed
        if row.n < SPREAD:
            row.postpone, row.work_at, row.close_at = True, (), None
        owed = (before, store, 3 * nb + index) if row.postpone else None
        yield row
        store = before[1] if before[0] == LAST else None
        before = (LAST, r)
    yield Row(LAST, SPREAD + 1, (nb - 2) - SPREAD, (LAST, SPREAD), store)
    with eng.Fori(SPREAD + 2, nb - CUT[LAST]) as r:
        yield Row(LAST, r, (nb - 1) - r, (LAST, r - 1), r - 2)
    for n in range(CUT[LAST] - 1, SPREAD - 1, -1):
        yield Row(LAST, nb - 1 - n, n, (LAST, nb - 2 - n), nb - 3 - n)


def last_head(nb):
    return [r for k in range(SPREAD) for r in (k, nb - 1 - k)]


def blocks(eng, row):
    first = max(2, row.use_at + 1)
    if isinstance(row.n, int) and row.n <= first:
        yield from range(max(row.n, row.use_at + 1))
        return
    yield from range(first)
    with eng.Fori(first, row.n) as k:
        yield k


def at(k, position):
    return isinstance(k, int) and isinstance(position, int) and k == position


def column(row, k, nb):
    if row.sweep == DOWN:
        return (row.r + 1 + k) % nb
    if row.sweep == UP2:
        return (nb - 1) - k
    if row.sweep == DOWN3:
        return k
    return row.r + 1 + k


class Count:

    def __init__(self, eng, name, top, start=0):
        self.eng, self.top = eng, top
        self.reg = eng.alloc_register(name)
        eng.reg_mov(self.reg, start)

    def value(self):
        return self.eng.snap(self.reg, min_val=0, max_val=self.top)

    def add(self, by=1):
        self.eng.reg_add(self.reg, self.reg, by)


def chebyshev_program(nc: bass.Bass, a_blocks, x_rows, x_cols, weights, bias, out):
    nb, _, _, _, wide = a_blocks.shape
    tiles = wide // P
    half = tiles // 2
    feat = x_cols.shape[0]
    off_diagonal = nb * (nb - 1)
    assert feat == 64 and wide == 512 and (off_diagonal // 2) % SLOTS == 0
    before_last = off_diagonal * 2 + 2 * nb
    many = 4 * nb * nb * tiles
    last_row = nb - 1 - SPREAD

    with ExitStack() as ctx:
        def sb(name, shape, dtype=F32):
            return ctx.enter_context(nc.sbuf_tensor(name, shape, dtype))

        def psum(name, shape):
            return ctx.enter_context(nc.psum_tensor(name, shape, F32))

        def sem(name):
            return ctx.enter_context(nc.semaphore(name))

        a_ring = sb("a_ring", [P, SLOTS, tiles * wide])
        a_diag = sb("a_diag", [P, 2, tiles * wide])
        a_high = sb("a_high", [P, 2, tiles * wide], F32R)
        a_low = sb("a_low", [P, 2, tiles * wide], F32R)
        operand = sb("operand", [P, nb, tiles, 2, 2, feat], F32R)
        staged = sb("staged", [P, tiles, 2, 2 * feat], F32R)
        staged_again = sb("staged_again", [P, tiles, 2, feat])
        staged_last = sb("staged_last", [P, half, 2, feat])
        cols = sb("cols", [P, nb, wide])
        natural = sb("natural", [P, nb, tiles, feat])
        turn_in = sb("turn_in", [P, wide])
        zero = sb("zero", [P, P])
        bias_all = sb("bias_all", [P, feat])
        turn_w = sb("turn_w", [P, 4, P])
        h = sb("h", [P, tiles, feat])
        sq = sb("sq", [P, tiles, feat])
        stat = sb("stat", [P, 2, tiles])
        eps = sb("eps", [P, 1])

        acc = psum("acc", [P, 2, wide])
        turned = psum("turned", [P, tiles, P])

        s_x = [sem(f"s_x{c}") for c in range(4)]
        s_const = sem("s_const")
        s_ident = sem("s_ident")
        s_opinit = sem("s_opinit")
        s_slot = [sem(f"s_slot{i}") for i in range(SLOTS)]
        s_landed = sem("s_landed")
        s_diag = sem("s_diag")
        s_high = sem("s_high")
        s_low = sem("s_low")
        s_high_d = sem("s_high_d")
        s_low_d = sem("s_low_d")
        s_staged_a = sem("s_staged_a")
        s_staged_p = sem("s_staged_p")
        s_tile = sem("s_tile")
        s_again_in = sem("s_again_in")
        s_again = sem("s_again")
        s_zeroed = sem("s_zeroed")
        s_turnin = sem("s_turnin")
        s_turned = sem("s_turned")
        s_result = sem("s_result")
        s_bank = sem("s_bank")
        s_var = sem("s_var")
        s_std = sem("s_std")
        s_out = sem("s_out")

        def staging(sweep, col, t):
            if sweep == LAST:
                return (staged[:, t, 0].rearrange("p (a f) -> p a f", a=2),
                        operand[:, col, t, :, NOW[LAST], :])
            return (staged[:, t].rearrange("p a f -> p (a f)"),
                    operand[:, col, t].rearrange("p a s f -> p (a s f)"))

        block = ctx.enter_context(nc.Block())

        @block.sync
        def _(sp):
            quads = Count(sp, "quads", many)
            former = Count(sp, "former", many)
            former_last = Count(sp, "former_last", many)
            row_at, col_at, edge = (sp.alloc_register(name) for name in ("row_at", "col_at", "edge"))
            sp.reg_mov(row_at, 0)
            sp.reg_mov(col_at, 1)

            def step(sweep):
                if sweep == DOWN:
                    sp.reg_add(col_at, col_at, 1)
                    sp.reg_alu(col_at, col_at, nb, op=ALU.mod)
                    sp.reg_alu(edge, col_at, row_at, op=ALU.is_equal)
                    sp.reg_add(row_at, row_at, edge)
                    sp.reg_add(col_at, col_at, edge)
                    sp.reg_add(col_at, col_at, edge)
                    sp.reg_alu(col_at, col_at, nb, op=ALU.mod)
                elif sweep == UP2:
                    sp.reg_alu(col_at, col_at, 1, op=ALU.subtract)
                    sp.reg_alu(edge, col_at, row_at, op=ALU.is_equal)
                    sp.reg_alu(row_at, row_at, edge, op=ALU.subtract)
                    sp.reg_alu(row_at, row_at, 0, op=ALU.max)
                    sp.reg_alu(edge, edge, nb, op=ALU.mult)
                    sp.reg_alu(col_at, col_at, edge, op=ALU.max)
                    sp.reg_alu(col_at, col_at, nb - 1, op=ALU.min)
                elif sweep == DOWN3:
                    sp.reg_add(col_at, col_at, 1)
                    sp.reg_alu(edge, col_at, row_at, op=ALU.is_equal)
                    sp.reg_add(row_at, row_at, edge)
                    sp.reg_alu(edge, edge, -nb, op=ALU.mult)
                    sp.reg_add(col_at, col_at, edge)
                    sp.reg_alu(col_at, col_at, 0, op=ALU.max)
                else:
                    sp.reg_add(col_at, col_at, 1)
                    sp.reg_alu(edge, col_at, nb, op=ALU.is_equal)
                    sp.reg_add(row_at, row_at, edge)
                    sp.reg_alu(col_at, col_at, nb, op=ALU.mod)
                    sp.reg_alu(edge, edge, row_at, op=ALU.mult)
                    sp.reg_add(col_at, col_at, edge)
                    sp.reg_alu(edge, edge, 1, op=ALU.min)
                    sp.reg_add(col_at, col_at, edge)

            def quad(sweep, first=False, by_tensor=False, places=None):
                q, f = quads.value(), (former_last if by_tensor else former).value()
                for s in range(SLOTS):
                    if not first or s == SLOTS - 1:
                        oldest = (s + 1) % SLOTS
                        sp.wait_ge(s_slot[oldest], 16 * (q if oldest else q + 1))
                        sp.sem_inc(s_landed, 1)
                    if by_tensor:
                        sp.wait_ge(s_tile, f * (SLOTS * tiles) + ((before_last + s) * tiles + half + 1))
                    elif not first:
                        sp.wait_ge(s_low, f * (SLOTS * 2) + (s + 1) * 2)
                    if places:
                        r, c = places[s]
                    else:
                        r = sp.snap(row_at, min_val=0, max_val=nb - 1)
                        c = sp.snap(col_at, min_val=0, max_val=nb - 1)
                    sp.dma_start(a_ring[:, s, :],
                                 a_blocks[r, c].rearrange("p t i -> p (t i)")).then_inc(s_slot[s], 16)
                    if not places:
                        step(sweep)
                quads.add()
                if by_tensor:
                    former_last.add()
                elif not first:
                    former.add()

            quad(DOWN, first=True)
            with sp.Fori(1, off_diagonal // SLOTS) as _q:
                quad(DOWN)
            triangle = off_diagonal // 2 // SLOTS
            for sweep, start in ((UP2, (nb - 2, nb - 1)), (DOWN3, (1, 0))):
                sp.reg_mov(row_at, start[0])
                sp.reg_mov(col_at, start[1])
                with sp.Fori(0, triangle) as _q:
                    quad(sweep)
            places = [(r, c) for r in last_head(nb) for c in range(r + 1, nb)]
            rest = -len(places) % SLOTS
            places += [(SPREAD, SPREAD + 1 + k) for k in range(rest)]
            for q in range(0, len(places), SLOTS):
                quad(LAST, by_tensor=q > 0, places=places[q:q + SLOTS])
            sp.reg_mov(row_at, SPREAD)
            sp.reg_mov(col_at, SPREAD + 1 + rest)
            with sp.Fori(len(places) // SLOTS, triangle) as _q:
                quad(LAST, by_tensor=True)
            for s in range(1, SLOTS):
                sp.wait_ge(s_slot[s], 16 * (off_diagonal // SLOTS + 3 * triangle))
                sp.sem_inc(s_landed, 1)
            sp.wait_ge(s_out, 16 * nb)

        @block.scalar
        def _(act):
            for c in range(4):
                part = slice(c * nb // 4, (c + 1) * nb // 4)
                act.dma_start(natural[:, part], x_rows[:, part]).then_inc(s_x[c], 16)
            act.dma_start(cols[feat:P], x_cols.rearrange("f (b i) -> f b i", i=wide)).then_inc(s_const, 16)
            act.dma_start(bias_all[:, :], bias.rearrange("(a f) -> a f", a=1).broadcast_to([P, feat])
                          ).then_inc(s_const, 16)
            act.wait_ge(s_ident, 5)
            act.dma_start(turn_w[0:feat, 0, 0:feat], weights[1]).then_inc(s_const, 16)
            act.dma_start(turn_w[feat:P, 0, 0:feat], weights[0]).then_inc(s_const, 16)
            act.dma_start(turn_w[0:feat, 2, 0:feat], weights[3]).then_inc(s_const, 16)
            act.dma_start(turn_w[feat:P, 2, 0:feat], weights[2]).then_inc(s_const, 16)

            total = Count(act, "total", many)
            ring = Count(act, "ring", many)
            slot_no = Count(act, "slot_no", SLOTS - 1)
            loads = Count(act, "loads", many)
            closed = Count(act, "closed", many)
            norms = Count(act, "norms", many)
            freed = Count(act, "freed", many)
            tile_freed = Count(act, "tile_freed", many)
            col_at = act.alloc_register("col_at")
            handled = [0]

            def round_block(sweep, source, ready, done):
                high = a_high[:, total.value() % 2, :]
                for g in range(SPLIT_HALVES[sweep]):
                    if handled[0] >= 2:
                        act.wait_ge(s_tile, freed.value() + (ORDER[sweep].index((g + 1) * half - 1) + 1))
                    if g == 0:
                        act.wait_ge(*ready())
                    part = slice(g * half * wide, (g + 1) * half * wide)
                    act.activation(high[:, part], source[:, part], ACT.Copy).then_inc(done, 1)
                if handled[0] >= 2:
                    freed.add(tiles)

            def stage(sweep):
                col = act.snap(col_at, min_val=0, max_val=nb - 1)
                for t in range(half):
                    if handled[0] >= 1:
                        act.wait_ge(s_tile, tile_freed.value() + (ORDER[sweep].index(t) + 1))
                    place, source = staging(sweep, col, t)
                    act.activation(place, source, ACT.Copy).then_inc(s_staged_a, 1)
                if handled[0] >= 1:
                    tile_freed.add(tiles)
                total.add()
                handled[0] += 1

            def deviation():
                norms.add()
                act.wait_ge(s_var, norms.value())
                act.activation(stat[:, 1, :], stat[:, 1, :], ACT.Sqrt, scale=1.0 / feat, bias=eps[:, 0:1]
                               ).then_inc(s_std, 1)

            def store(r, count):
                act.wait_ge(s_result, count)
                act.dma_start(out[r], natural[:, r]).then_inc(s_out, 16)

            def handle_diagonal(row):
                place = loads.value() % 2
                loads.add()
                count = loads.value()
                round_block(row.sweep, a_diag[:, place, :], lambda: (s_diag, count * 16), s_high_d)
                act.reg_mov(col_at, row.r)
                stage(row.sweep)

            def wait_for_result():
                act.wait_ge(s_result, closed.value())

            for row in rows(act, nb):
                for k in blocks(act, row):
                    needs_deviation = at(k, row.close_at) and row.before and row.before[0] in (DOWN3, LAST)
                    if needs_deviation and not (row.round_first and not at(k, row.n)):
                        deviation()
                    if row.owed and at(k, OWED_STEPS):
                        deviation()
                        if row.owed[1] is not None:
                            store(row.owed[1], closed.value())
                        closed.add()
                    use = at(k, row.use_at) and row.before and not row.postpone
                    if use and row.store is not None:
                        store(row.store, closed.value())
                    if use:
                        closed.add()
                    if at(k, row.n):
                        if use and row.before[0] != LAST:
                            wait_for_result()
                        break
                    if at(k, row.diagonal_at):
                        handle_diagonal(row)
                    if handled[0] == 0:
                        act.wait_ge(s_opinit, 1)
                    slot = slot_no.value()
                    round_block(row.sweep, a_ring[:, slot, :], lambda: (s_landed, ring.value() + 1), s_high)
                    if needs_deviation and row.round_first:
                        deviation()
                    if use and row.before[0] != LAST:
                        wait_for_result()
                    act.reg_mov(col_at, column(row, k, nb))
                    stage(row.sweep)
                    ring.add()
                    slot_no.add()
                    act.reg_alu(slot_no.reg, slot_no.reg, SLOTS, op=ALU.mod)
                if row.diagonal and row.diagonal_at is None:
                    handle_diagonal(row)
            deviation()
            store(last_row - 1, 4 * nb - 1)
            store(last_row, 4 * nb)

        @block.gpsimd
        def _(pool):
            def load_diagonal(r, place):
                pool.dma_start(a_diag[:, place, :], a_blocks[r, r].rearrange("p t i -> p (t i)")
                               ).then_inc(s_diag, 16)

            nc.gpsimd.memset(zero[:], 0.0)
            nc.gpsimd.memset(eps[:], EPS)
            nc.gpsimd.memset(staged_again[:], 0.0)
            nc.gpsimd.memset(staged_last[:], 0.0)
            nc.gpsimd.memset(turn_w[:], 0.0).then_inc(s_ident, 1)
            pool.wait_ge(s_ident, 1)
            for kind, sides in ((DOWN, (0,)), (UP2, (1,)), (LAST, (0, 1))):
                for side in sides:
                    rows_of_side = slice(side * feat, (side + 1) * feat)
                    nc.gpsimd.affine_select(out=turn_w[rows_of_side, kind, feat:P],
                                            in_=turn_w[rows_of_side, kind, feat:P],
                                            compare_op=ALU.not_equal, fill=1.0, base=0,
                                            pattern=[[-1, feat]], channel_multiplier=1).then_inc(s_ident, 1)
            closed = Count(pool, "closed", many)
            tile_freed = Count(pool, "tile_freed", many)
            loads = Count(pool, "loads", many)
            rounded = Count(pool, "rounded", many)
            agains = Count(pool, "agains", many)
            col_at = pool.alloc_register("col_at")
            handled = [0]
            pool.wait_ge(s_ident, 5)
            load_diagonal(0, 0)
            pool.wait_ge(s_opinit, 1)

            def wait_for_result():
                pool.wait_ge(s_result, closed.value())

            def place_free(row):
                waits = [lambda: (s_high_d, rounded.value() + 2)]
                if row.before:
                    waits.append(lambda: (s_again, agains.value() + 1 if row.before[0] in DIAGONAL else nb))
                return waits

            def stage(sweep, more=()):
                col = pool.snap(col_at, min_val=0, max_val=nb - 1)
                for t in range(half, tiles):
                    if handled[0] >= 1:
                        pool.wait_ge(s_tile, tile_freed.value() + (ORDER[sweep].index(t) + 1))
                    if t == tiles - 1:
                        for wait in more:
                            pool.wait_ge(*wait())
                    if sweep == LAST:
                        place, source = staged_last[:, t - half, 1, :], natural[:, col, t, :]
                    else:
                        place, source = staging(sweep, col, t)
                    nc.gpsimd.tensor_copy(place, source).then_inc(s_staged_p, 1)
                if handled[0] >= 1:
                    tile_freed.add(tiles)
                handled[0] += 1

            for row in rows(pool, nb):
                for k in blocks(pool, row):
                    if at(k, row.use_at) and row.before:
                        closed.add()
                    if at(k, row.n):
                        break
                    if at(k, row.diagonal_at):
                        pool.reg_mov(col_at, row.r)
                        stage(row.sweep)
                    pool.reg_mov(col_at, column(row, k, nb))
                    if at(k, row.use_at) and row.before and row.before[0] != LAST:
                        wait_for_result()
                    stage(row.sweep, place_free(row) if at(k, row.diagonal_at) else ())
                if row.diagonal and row.diagonal_at is None:
                    pool.reg_mov(col_at, row.r)
                    if at(row.n, 0) and row.before:
                        wait_for_result()
                    stage(row.sweep, place_free(row))
                if row.diagonal:
                    rounded.add(2)
                    if row.before:
                        agains.add()
                    loads.add()
                    if not (row.sweep == DOWN3 and at(row.r, nb - 1)):
                        pool.reg_mov(col_at, (row.r + 1) % nb)
                        load_diagonal(pool.snap(col_at, min_val=0, max_val=nb - 1), loads.value() % 2)

        @block.tensor
        def _(pe):
            total = Count(pe, "total", many)
            slot_no = Count(pe, "slot_no", SLOTS - 1)
            blocks_landed = Count(pe, "blocks_landed", many, start=off_diagonal * 2)
            ring = Count(pe, "ring", many)
            diag = Count(pe, "diag", many)
            agains = Count(pe, "agains", many)
            row_no = Count(pe, "row_no", many)
            banks = Count(pe, "banks", many, start=1)

            def multiply(sweep, bank, start, on_diagonal=False):
                x = total.value()
                high, low = a_high[:, x % 2, :], a_low[:, x % 2, :]
                count, split = (diag, s_low_d) if on_diagonal else (ring, s_low)
                y = count.value()
                if sweep == LAST:
                    pe.wait_ge(s_landed, blocks_landed.value() + 1)
                    blocks_landed.add()
                for t in ORDER[sweep]:
                    g = t // half
                    if t % half == 0 and g < SPLIT_HALVES[sweep]:
                        pe.wait_ge(split, y + (g + 1))
                    pe.wait_ge(s_staged_a if t < half else s_staged_p, x * half + (t % half + 1))
                    part = slice(t * wide, (t + 1) * wide)
                    if g < SPLIT_HALVES[sweep]:
                        passes = [(staged[:, t, 0, :], high[:, part]), (staged[:, t, 0, :], low[:, part]),
                                  (staged[:, t, 1, :], high[:, part])]
                        if sweep == LAST:
                            passes.pop()
                    else:
                        passes = [(staged_last[:, t - half].rearrange("p s f -> p (s f)"),
                                   a_ring[:, slot_no.value(), part])]
                    for n, (stationary, moving) in enumerate(passes):
                        last = nc.tensor.matmul(acc[:, bank, :], stationary, moving,
                                                start=start and t == ORDER[sweep][0] and n == 0, stop=False,
                                                skip_group_check=True)
                    last.then_inc(s_tile, 1)
                total.add()
                count.add(SPLIT_HALVES[sweep])
                if not on_diagonal:
                    slot_no.add()
                    pe.reg_alu(slot_no.reg, slot_no.reg, SLOTS, op=ALU.mod)

            def multiply_again(bank):
                place = agains.value() % 2
                agains.add()
                pe.wait_ge(s_again_in, agains.value())
                for t in range(tiles):
                    last = nc.tensor.matmul(acc[:, bank, :], staged_again[:, t].rearrange("p s f -> p (s f)"),
                                            a_diag[:, place, t * wide:(t + 1) * wide],
                                            start=False, stop=False, skip_group_check=True)
                last.then_inc(s_again, 1)

            def turn(sweep, number):
                pe.wait_ge(s_turnin, number)
                part = {DOWN: slice(0, P), DOWN3: slice(0, feat)}.get(sweep, slice(feat, P))
                for t in range(tiles):
                    last = nc.tensor.matmul(turned[:, t, part], turn_in[:, t * P:(t + 1) * P],
                                            turn_w[:, sweep, part], start=True, stop=True)
                last.then_inc(s_turned, 1)

            for row in rows(pe, nb):
                number = row_no.value()
                bank, bank_before = number % 2, (number + 1) % 2
                if row.before:
                    if not (row.before[0] == LAST and not at(row.before[1], 0)):
                        pe.wait_ge(s_bank, banks.value())
                    banks.add()
                for k in blocks(pe, row):
                    if at(k, row.turn_at) and row.before:
                        turn(row.before[0], number)
                    if at(k, row.diagonal_at):
                        multiply(row.sweep, bank, at(k, 0), on_diagonal=True)
                    if at(k, row.close_at) and row.before and row.before[0] in DIAGONAL:
                        multiply_again(bank_before)
                    if at(k, row.n):
                        break
                    multiply(row.sweep, bank, at(k, 0) and row.diagonal_at != 0)
                if row.diagonal and row.diagonal_at is None:
                    multiply(row.sweep, bank, at(row.n, 0), on_diagonal=True)
                elif at(row.n, 0):
                    for t in range(tiles):
                        last = nc.tensor.matmul(acc[:, bank, t * P:(t + 1) * P], zero[:], zero[:], start=True,
                                                stop=False, skip_group_check=True)
                    last.then_inc(s_zeroed, 1)
                row_no.add()
            turn(LAST, 4 * nb)

        @block.vector
        def _(dve):
            nc.vector.memset(operand[:, :, :, :, 1, :].bitcast(F32), 0.0)
            for c in range(4):
                part = slice(c * nb // 4, (c + 1) * nb // 4)
                dve.wait_ge(s_x[c], 16)
                nc.vector.tensor_copy(operand[:, part, :, 0, 0, :], natural[:, part])
                dve.drain()
                last = nc.vector.tensor_tensor(operand[:, part, :, 1, 0, :], natural[:, part],
                                               operand[:, part, :, 0, 0, :], ALU.subtract)
            last.then_inc(s_opinit, 1)
            dve.sem_inc(s_bank, 1)

            total = Count(dve, "total", many)
            ring = Count(dve, "ring", many)
            slot_no = Count(dve, "slot_no", SLOTS - 1)
            diag = Count(dve, "diag", many)
            loads = Count(dve, "loads", many)
            agains = Count(dve, "agains", many)
            row_no = Count(dve, "row_no", many)
            norms = Count(dve, "norms", many)
            halves = (slice(0, feat), slice(feat, P))

            def split_block(sweep, source, count, ready, done):
                x, y = total.value(), count.value()
                for g in range(SPLIT_HALVES[sweep]):
                    part = slice(g * half * wide, (g + 1) * half * wide)
                    dve.wait_ge(ready, y + (g + 1))
                    nc.vector.tensor_tensor(a_low[:, x % 2, part], source[:, part],
                                            a_high[:, x % 2, part], ALU.subtract).then_inc(done, 1)
                total.add()
                count.add(SPLIT_HALVES[sweep])

            def take_mean():
                nc.vector.tensor_reduce(out=stat[:, 0, :], in_=h[:], op=ALU.add, axis=AX_X)
                dve.drain()

            def center():
                nc.vector.scalar_tensor_tensor(out=h[:],
                                               in0=stat[:, 0, :].unsqueeze(2).broadcast_to([P, tiles, feat]),
                                               scalar=-1.0 / feat, in1=h[:], op0=ALU.mult, op1=ALU.add)
                dve.drain()

            def square():
                nc.vector.tensor_tensor(sq[:], h[:], h[:], ALU.mult)
                dve.drain()
                nc.vector.tensor_reduce(out=stat[:, 1, :], in_=sq[:], op=ALU.add, axis=AX_X
                                        ).then_inc(s_var, 1)
                norms.add()

            def normalise(r):
                dve.wait_ge(s_std, norms.value())
                nc.vector.reciprocal(stat[:, 0, :], stat[:, 1, :])
                dve.drain()
                return nc.vector.tensor_tensor(natural[:, r], h[:],
                                               stat[:, 0, :].unsqueeze(2).broadcast_to([P, tiles, feat]),
                                               ALU.mult)

            def gather_result(sweep, r, bank, sums, count):
                now = NOW[sweep]
                mine, other = halves[now], halves[1 - now]
                if sweep in DIAGONAL:
                    nc.vector.tensor_copy(turn_in[other], cols[other, r])
                dve.wait_ge(sums, count)
                if sweep == DOWN:
                    nc.vector.tensor_copy(turn_in[mine], acc[mine, bank]).then_inc(s_turnin, 1)
                elif sweep == LAST:
                    nc.vector.tensor_copy(turn_in[other], acc[other, bank])
                    nc.vector.tensor_tensor(turn_in[mine], acc[mine, bank], cols[mine, r], ALU.add
                                            ).then_inc(s_turnin, 1)
                else:
                    nc.vector.scalar_tensor_tensor(out=turn_in[mine], in0=acc[mine, bank], scalar=2.0,
                                                   in1=cols[mine, r], op0=ALU.mult, op1=ALU.add
                                                   ).then_inc(s_turnin, 1)

            def clear_operand(r):
                nc.vector.tensor_copy(operand[:, r, :, :, 1, :],
                                      zero[:, 0:feat].unsqueeze(1).unsqueeze(1).broadcast_to([P, tiles, 2, feat]))

            def store_operand(r, side, value):
                nc.vector.tensor_copy(operand[:, r, :, 0, side, :], value)
                dve.drain()
                return nc.vector.tensor_tensor(operand[:, r, :, 1, side, :], value,
                                               operand[:, r, :, 0, side, :], ALU.subtract)

            def work_on(step, sweep, r, number):
                by_rows, share = turned[:, :, feat:P], turned[:, :, 0:feat]
                if step == 0 and sweep in (DOWN3, LAST):
                    dve.wait_ge(s_turned, number)
                if sweep == DOWN3:
                    if step == 0:
                        nc.vector.tensor_tensor(h[:], natural[:, r], share, ALU.add)
                        dve.drain()
                        take_mean()
                    elif step == 1:
                        center()
                    else:
                        square()
                elif sweep == LAST:
                    outer = stat[:, 0, :]
                    if step == 0:
                        nc.vector.tensor_tensor(sq[:], natural[:, r], by_rows, ALU.mult)
                        nc.vector.tensor_scalar(h[:], natural[:, r], 1.0 - B_CONST, F_CONST, ALU.mult, ALU.add)
                        dve.drain()
                        nc.vector.tensor_reduce(out=outer, in_=sq[:], op=ALU.add, axis=AX_X)
                        dve.drain()
                    elif step == 1:
                        nc.vector.scalar_tensor_tensor(
                            out=h[:], in0=outer.unsqueeze(2).broadcast_to([P, tiles, feat]),
                            scalar=-R_CONST, in1=h[:], op0=ALU.mult, op1=ALU.add)
                        dve.drain()
                    else:
                        take_mean()
                        center()
                        square()

            def store_result(sweep, r, number):
                side = 1 - NOW[sweep]
                by_rows, share = turned[:, :, feat:P], turned[:, :, 0:feat]
                if sweep in (DOWN, UP2):
                    dve.wait_ge(s_turned, number)
                    if sweep == DOWN:
                        nc.vector.tensor_copy(staged_again[:, :, 1, :], by_rows).then_inc(s_again_in, 1)
                    store_operand(r, side, by_rows).then_inc(s_result, 1)
                    if sweep == DOWN:
                        nc.vector.tensor_tensor(natural[:, r], natural[:, r], share, ALU.add)
                elif sweep == DOWN3:
                    normalise(r)
                    dve.drain()
                    nc.vector.tensor_copy(staged_again[:, :, 1, :], natural[:, r]).then_inc(s_again_in, 1)
                    store_operand(r, side, natural[:, r]).then_inc(s_result, 1)
                else:
                    normalise(r).then_inc(s_result, 1)

            def keep_sums(sweep, r, bank):
                now = NOW[sweep]
                mine, other = halves[now], halves[1 - now]
                if sweep in (DOWN, UP2):
                    nc.vector.scalar_tensor_tensor(out=cols[other, r], in0=acc[other, bank], scalar=2.0,
                                                   in1=cols[other, r], op0=ALU.mult, op1=ALU.subtract)
                    nc.vector.tensor_copy(cols[mine, r], turn_in[mine]).then_inc(s_bank, 1)
                elif sweep == DOWN3:
                    nc.vector.tensor_copy(cols[other, r], acc[other, bank]).then_inc(s_bank, 1)
                else:
                    dve.sem_inc(s_bank, 1)

            for row in rows(dve, nb):
                number = row_no.value()
                bank_before = (number + 1) % 2
                blocks_before = total.value()

                def split_ring_block():
                    split_block(row.sweep, a_ring[:, slot_no.value(), :], ring, s_high, s_low)
                    slot_no.add()
                    dve.reg_alu(slot_no.reg, slot_no.reg, SLOTS, op=ALU.mod)

                def keep_row_before():
                    if row.before[0] in DIAGONAL:
                        agains.add()
                        dve.wait_ge(s_again, agains.value())
                    keep_sums(*row.before, bank_before)

                def split_diagonal():
                    split_block(row.sweep, a_diag[:, loads.value() % 2, :], diag, s_high_d, s_low_d)
                    loads.add()

                for k in blocks(dve, row):
                    if at(k, 0) and row.sweep == DOWN3 and not (at(row.r, 0) or at(row.r, nb - 1)):
                        clear_operand(row.r + 1)
                    if not row.before and isinstance(k, int) and 0 < k <= 4:
                        if k == 1:
                            dve.wait_ge(s_const, 6 * 16)
                        part = slice((k - 1) * nb // 4, k * nb // 4)
                        nc.vector.tensor_tensor(
                            natural[:, part], natural[:, part],
                            bias_all[:].unsqueeze(1).unsqueeze(1).broadcast_to([P, nb // 4, tiles, feat]), ALU.add)
                    if at(k, 0) and at(row.diagonal_at, 0):
                        split_diagonal()
                    if at(k, row.turn_at) and row.before:
                        sweep, before = row.before
                        dve.drain()
                        no_block = sweep in (UP2, LAST) and at(before, nb - 1)
                        sums, count = (s_zeroed, 1 if sweep == UP2 else 2) if no_block else (s_tile, blocks_before * tiles)
                        gather_result(sweep, before, bank_before, sums, count)
                        if row.sweep == DOWN3 and at(row.r, 0):
                            clear_operand(0)
                            clear_operand(1)
                        if at(k, row.diagonal_at) and k > 0:
                            split_diagonal()
                    elif at(k, row.diagonal_at):
                        split_diagonal()
                    if at(k, row.close_at) and row.split_first:
                        split_ring_block()
                    if row.owed and isinstance(k, int) and k < OWED_STEPS:
                        work_on(k, *row.owed[0], row.owed[2])
                    if row.owed and at(k, OWED_STEPS):
                        store_result(*row.owed[0], row.owed[2])
                        dve.drain()
                    for step, position in enumerate(row.work_at):
                        if at(k, position):
                            work_on(step, *row.before, number)
                    if at(k, row.close_at) and row.before:
                        store_result(*row.before, number)
                    if at(k, row.n):
                        break
                    if not (at(k, row.close_at) and row.split_first):
                        split_ring_block()
                    if at(k, row.keep_at):
                        keep_row_before()
                if row.diagonal and row.diagonal_at is None:
                    split_diagonal()
                if row.before and row.keep_at is None:
                    keep_row_before()
                row_no.add()
            dve.drain()
            gather_result(LAST, last_row, (4 * nb + 1) % 2, s_tile, total.value() * tiles)
            for step in range(3):
                work_on(step, LAST, last_row, 4 * nb)
            store_result(LAST, last_row, 4 * nb)


def kernel(x, adj, L0_gnn_weights, L0_gnn_bias, L1_gnn_t):
    import numpy as np
    import concourse.bacc as bacc
    from concourse.bass_utils import run_bass_kernel_spmd

    n, feat = x.shape
    wide = 512
    nb, tiles = n // wide, wide // P
    adj, x = np.asarray(adj), np.asarray(x)
    a_blocks = np.ascontiguousarray(
        adj.reshape(nb, wide, nb, tiles, P).transpose(0, 2, 4, 3, 1))
    x_rows = np.ascontiguousarray(x.reshape(nb, tiles, P, feat).transpose(2, 0, 1, 3))
    arrays = {"a_blocks": a_blocks, "x_rows": x_rows, "x_cols": np.ascontiguousarray(x.T),
              "weights": np.ascontiguousarray(L0_gnn_weights), "bias": np.ascontiguousarray(L0_gnn_bias)}
    nc = bacc.Bacc("TRN2", target_bir_lowering=False, num_devices=1)
    args = [nc.dram_tensor(k, v.shape, F32, kind="ExternalInput").ap() for k, v in arrays.items()]
    out = nc.dram_tensor("out", (nb, P, tiles, feat), F32, kind="ExternalOutput").ap()
    chebyshev_program(nc, *args, out)
    result = run_bass_kernel_spmd(nc, [arrays], core_ids=[0])
    got = result.results[0]["out"]
    return np.ascontiguousarray(got.transpose(0, 2, 1, 3).reshape(n, feat))
```
